# Optimizing a Trainium2 kernel written in Bass

```python
import numpy as np
import jax
import jax.numpy as jnp

def _softmax(x, axis=-1):
    return jax.nn.softmax(x, axis=axis)

def _gelu(x):
    return jax.nn.gelu(x, approximate=True)

def _silu(x):
    return jax.nn.silu(x)

def _sigmoid(x):
    return jax.nn.sigmoid(x)

def _layernorm(x, axis=-1, eps=1e-05):
    m = jnp.mean(x, axis=axis, keepdims=True)
    v = jnp.var(x, axis=axis, keepdims=True)
    return (x - m) / jnp.sqrt(v + eps)

def _scatter_add(tgt, idx, src, axis=0):
    return tgt.at[idx].add(src)

def _segment_sum(src, seg, n):
    return jax.ops.segment_sum(src, seg, n)
kernel_name = 'mk_flamingo_gated_d1_seqx_r8_25bc42'

def setup_inputs(seed: int=0):
    np.random.seed(seed)
    _w = jnp.asarray

    def _rec_inputs():
        import jax
        import jax.numpy as jnp
        _rk = jax.random.key(seed)
        x = 7.22e-05 + 1 * jax.random.normal(jax.random.fold_in(_rk, 1), (64, 64, 256), jnp.float32)
        _lenS = 64 - jax.random.randint(jax.random.fold_in(_rk, 7), (64,), 0, max(1, 64 // 4) + 1, jnp.int32)
        _lenS2 = 64 - jax.random.randint(jax.random.fold_in(_rk, 8), (64,), 0, max(1, 64 // 4) + 1, jnp.int32)
        _ctx_2048P = jax.random.normal(jax.random.fold_in(_rk, 11), (64, 16, 256), jnp.float32)
        _ctx_2048c = jax.random.dirichlet(jax.random.fold_in(_rk, 511), 0.3 * jnp.ones((16,), jnp.float32), (64, 64))
        _ctx_2048t = jnp.einsum('bsk,bkd->bsd', _ctx_2048c, _ctx_2048P)
        _ctx_2048t = _ctx_2048t * jax.lax.rsqrt(jnp.mean(jnp.square(_ctx_2048t)) + 1e-12) * 0.953939
        ctx_2048 = 4.13588e-05 + 0.999923 * (_ctx_2048t + 0.3 * jax.random.normal(jax.random.fold_in(_rk, 611), (64, 64, 256), jnp.float32))
        _g = jax.random.normal(jax.random.fold_in(_rk, 9001), (2, 1), jnp.float32)
        _g = jnp.sign(_g) * jnp.maximum(jnp.abs(_g), 1.0) + (_g == 0) * 1.0
        g_xattn = _g[0]
        g_ffn = _g[1]
        return (x, ctx_2048, g_xattn, g_ffn)
    x, ctx_2048, g_xattn, g_ffn = _rec_inputs()

    def _L0_xattn_setup():
        import jax, jax.numpy as jnp
        import numpy as np
        N_HEAD = 8
        key = jax.random.key(seed)
        k1, k2, k3 = jax.random.split(key, 3)
        B, D, L = (4, 128, 256)
        q = jax.random.normal(k1, (B, D, L), dtype=jnp.float32)
        k = jax.random.normal(k2, (B, D, L), dtype=jnp.float32)
        v = jax.random.normal(k3, (B, D, L), dtype=jnp.float32)
        gamma = jnp.ones((), dtype=jnp.float32)
        return {'q': q, 'k': k, 'v': v, 'gamma': gamma}
    _L0_xattn_all = _L0_xattn_setup()
    _L0_xattn_in = {k: v for k, v in _L0_xattn_all.items() if k in ('gamma',)}
    del _L0_xattn_all

    def _L0_ffn_setup():
        import jax, jax.numpy as jnp
        import numpy as np
        TOP_K = 8

        def _masked_routing(router_logits):
            T, E = router_logits.shape
            sel_w, sel_e = jax.lax.top_k(router_logits, TOP_K)
            sel_w = jax.nn.softmax(sel_w.astype(jnp.float32), axis=1)
            rows = jnp.arange(T)[:, None]
            masked = jnp.zeros((T, E), dtype=jnp.float32).at[rows, sel_e].set(sel_w)
            count = jnp.zeros((E,), dtype=jnp.int32).at[sel_e.reshape(-1)].add(1)
            return (masked, count)
        key = jax.random.key(seed)
        k1, k2, k3, k4, k5 = jax.random.split(key, 5)
        B, S, H, E, I = (1, 256, 256, 32, 96)
        return {'hidden_states': jax.random.normal(k1, (B, S, H), dtype=jnp.float32), 'gate_w': jax.random.normal(k2, (E, H), dtype=jnp.float32) * H ** (-0.5), 'w_gate_proj': jax.random.normal(k3, (E, I, H), dtype=jnp.float32) * H ** (-0.5), 'w_up_proj': jax.random.normal(k4, (E, I, H), dtype=jnp.float32) * H ** (-0.5), 'w_down_proj': jax.random.normal(k5, (E, H, I), dtype=jnp.float32) * I ** (-0.5)}
    _L0_ffn_all = _L0_ffn_setup()
    _L0_ffn_in = {k: v for k, v in _L0_ffn_all.items() if k in ('gate_w', 'w_gate_proj', 'w_up_proj', 'w_down_proj')}
    del _L0_ffn_all
    return {'x': x, 'ctx_2048': ctx_2048, 'g_xattn': g_xattn, 'g_ffn': g_ffn, 'L0_xattn_gamma': _L0_xattn_in['gamma'], 'L0_ffn_gate_w': _L0_ffn_in['gate_w'], 'L0_ffn_w_gate_proj': _L0_ffn_in['w_gate_proj'], 'L0_ffn_w_up_proj': _L0_ffn_in['w_up_proj'], 'L0_ffn_w_down_proj': _L0_ffn_in['w_down_proj']}

def reference(x, ctx_2048, g_xattn, g_ffn, L0_xattn_gamma, L0_ffn_gate_w, L0_ffn_w_gate_proj, L0_ffn_w_up_proj, L0_ffn_w_down_proj):
    import jax
    import jax.numpy as jnp

    def _L0_xattn_ref(q, k, v, gamma):
        import jax, jax.numpy as jnp
        import numpy as np
        N_HEAD = 8
        B, Dq, Lq = q.shape
        Dv, Lk = (v.shape[-2], v.shape[-1])
        h = N_HEAD
        dq = Dq // h
        dv = Dv // h
        qh = q.reshape(B, h, dq, Lq)
        kh = k.reshape(B, h, dq, Lk)
        vh = v.reshape(B, h, dv, Lk)
        scale = 1.0 / jnp.sqrt(jnp.asarray(dq, dtype=q.dtype))
        qk = jnp.einsum('bhdq,bhdl->bhql', qh, kh) * scale
        sm = jax.nn.softmax(qk, axis=-1)
        ret = jnp.einsum('bhql,bhdl->bhdq', sm, vh)
        ret = ret.reshape(B, Dv, Lq)
        return gamma * ret

    def _L0_ffn_ref(hidden_states, gate_w, w_gate_proj, w_up_proj, w_down_proj):
        import jax, jax.numpy as jnp
        import numpy as np
        TOP_K = 8

        def _masked_routing(router_logits):
            T, E = router_logits.shape
            sel_w, sel_e = jax.lax.top_k(router_logits, TOP_K)
            sel_w = jax.nn.softmax(sel_w.astype(jnp.float32), axis=1)
            rows = jnp.arange(T)[:, None]
            masked = jnp.zeros((T, E), dtype=jnp.float32).at[rows, sel_e].set(sel_w)
            count = jnp.zeros((E,), dtype=jnp.int32).at[sel_e.reshape(-1)].add(1)
            return (masked, count)
        B, S, H = hidden_states.shape
        x = hidden_states.reshape(-1, H)
        router_logits = x @ gate_w.T
        masked_w, _count = _masked_routing(router_logits)
        g = jnp.einsum('th,eih->tei', x, w_gate_proj)
        u = jnp.einsum('th,eih->tei', x, w_up_proj)
        h = jax.nn.silu(g) * u
        h = h * masked_w[:, :, None]
        out = jnp.einsum('tei,ehi->th', h, w_down_proj)
        return out.reshape(B, S, H)
    x = x + jnp.tanh(g_xattn[0]) * _L0_xattn_ref(_layernorm(x, axis=-1), ctx_2048, ctx_2048, L0_xattn_gamma)
    x = x + jnp.tanh(g_ffn[0]) * _L0_ffn_ref(_layernorm(x, axis=-1), L0_ffn_gate_w, L0_ffn_w_gate_proj, L0_ffn_w_up_proj, L0_ffn_w_down_proj)
    return x

_drawn_inputs = setup_inputs


def setup_inputs(seed=0):
    import zlib

    import numpy as np

    out = dict(_drawn_inputs(seed))
    spreads = {}
    factors = {}
    for name, (base, spread) in spreads.items():
        noise = np.random.default_rng([zlib.crc32(name.encode()), seed]).standard_normal(out[name].shape)
        drawn = base * np.exp(spread * noise) if base else spread * noise
        out[name] = jnp.asarray(drawn.astype(out[name].dtype))
    for name, factor in factors.items():
        out[name] = (out[name] * factor).astype(out[name].dtype)
    return out
```

```python
from contextlib import ExitStack

import concourse.bass as bass
from concourse import mybir

ALU = mybir.AluOpType
ACT = mybir.ActivationFunctionType
AX_X = mybir.AxisListType.X
F32 = mybir.dt.float32
F32R = mybir.dt.float32r

P = 128
BATCH, CH, L = 64, 64, 256
HEADS, DH = 8, 8
TOKENS = BATCH * CH
TILES = TOKENS // P
GROUPS = 4
JOBS = 4
EXPERTS, INNER, TOPK = 32, 96, 8
KT = L // P
WCOLS = EXPERTS * INNER
CHUNKS = WCOLS // P
WALL = 3 * KT * WCOLS
WSLICE = WALL // TILES
BLOCK = 512
BT = BLOCK // P
BLOCKS = TOKENS // BLOCK
EPS = 1e-5
WARM_UP = 12
SCALE = float(DH) ** -0.5
SELECTIONS = 2 * GROUPS + 2
OROWS = 16


def f32(ap):
    return ap.bitcast(F32)


def worked_out(engine, *values):
    return [v if isinstance(v, int) else engine.to_reg(v) for v in values]


def attention_phase(nc, x_rows, ctx_rows, v_cols, w_all, row_marks, select, eye, router, gates,
                    ident, router_sb, g3, consts_in, w_hi, w_lo, scratch):
    STEPS = TILES * GROUPS
    RING = 4
    HALF = P // 2
    Q_HI, Q_LO, K_BOTH = 0, GROUPS, 2 * GROUPS

    with ExitStack() as ctx:
        def sb(name, shape, dt=F32):
            return ctx.enter_context(nc.sbuf_tensor(name, shape, dt))

        def psum(name, shape):
            return ctx.enter_context(nc.psum_tensor(name, shape, F32))

        def sem(name):
            return ctx.enter_context(nc.semaphore(name))

        x2 = sb("x2", [P, 2, L])
        c2 = sb("c2", [P, 2, 2, L])
        v2 = sb("v2", [P, 2, KT, P])
        ws = sb("ws", [P, WSLICE])
        stats = sb("stats", [P, 2, 6])
        mv = sb("mv", [P, 2, 2])
        rstd = sb("rstd", [P, 2, 1])
        zero = sb("zero", [P, 1])
        half = sb("half", [P, 1])
        xn = sb("xn", [P, L])
        q_hi2 = sb("q_hi2", [P, 2, L], F32R)
        q_lo2 = sb("q_lo2", [P, 2, L], F32R)
        k_hl2 = sb("k_hl2", [P, 2, 2, L], F32R)
        sel = sb("sel", [P, SELECTIONS, P], F32R)
        qs4 = sb("qs4", [P, RING, L], F32R)
        ks4 = sb("ks4", [P, RING, L], F32R)
        ko4 = sb("ko4", [P, RING, 2, L], F32R)
        qm2 = sb("qm2", [P, 2, L], F32R)
        vs2 = sb("vs2", [P, 2, KT, 16, 32])
        mx = sb("mx", [P, 2, JOBS, KT])
        mt2 = sb("mt2", [P, 2, KT, P], F32R)
        ident_r = sb("ident_r", [P, P], F32R)
        marks = sb("marks", [P, 3])
        pr = sb("pr", [P, 4, 2, KT, L])
        sel_in = pr[:].rearrange("p a b c (d e) -> p (a b c d) e", e=P)[:, 0:SELECTIONS]
        os2 = sb("os2", [P, 2, GROUPS, L])

        s_ps = [psum(f"s_ps{i}", [P, KT, L]) for i in range(2)]
        st_ps = [psum(f"st_ps{i}", [P, 2, KT, L]) for i in range(2)]
        sums_ps = psum("sums_ps", [P, 2, L])
        pv_ps, q_ps = sums_ps[:, 0, :], sums_ps[:, 1, :]
        turn_ps = psum("turn_ps", [P, 2, L])
        mt_ps, k_ps = turn_ps[:, 0, :], turn_ps[:, 1, :]

        rows_in = [sem(f"rows_in{p}") for p in range(2)]
        v_in = [sem(f"v_in{p}") for p in range(2)]
        w_in = sem("w_in")
        sel_loaded = sem("sel_loaded")
        sel_done = sem("sel_done")
        mt_zero = sem("mt_zero")
        init = sem("init")
        stats_done = sem("stats_done")
        mv_done = sem("mv_done")
        veps_done = sem("veps_done")
        rstd_done = sem("rstd_done")
        xn_done = sem("xn_done")
        q_hi_done = sem("q_hi_done")
        q_lo_done = sem("q_lo_done")
        k_hi_done = sem("k_hi_done")
        k_lo_done = sem("k_lo_done")
        w_hi_done = sem("w_hi_done")
        w_lo_done = sem("w_lo_done")
        v_done = sem("v_done")
        q_stacked = sem("q_stacked")
        k_stacked = sem("k_stacked")
        qs_done = sem("qs_done")
        ks_done = sem("ks_done")
        ko_done = sem("ko_done")
        s_ready = sem("s_ready")
        max_done = sem("max_done")
        mneg_done = sem("mneg_done")
        mt_ready = sem("mt_ready")
        mt_done = sem("mt_done")
        qm_done = sem("qm_done")
        st_ready = sem("st_ready")
        exp_done = sem("exp_done")
        pv_ready = sem("pv_ready")
        os_done = sem("os_done")
        stored = [sem(f"stored{p}") for p in range(2)]

        block = ctx.enter_context(nc.Block())

        def tile_at(k, p, n):
            return k + (p + n) // 2, (p + n) % 2

        @block.sync
        def _(sp):
            def load_tile(k, p, early=False):
                t = 2 * k + p
                if not early:
                    used, = worked_out(sp, t - 1)
                    sp.wait_ge(consts_in, 64)
                    sp.wait_ge(q_lo_done, used)
                    sp.wait_ge(k_lo_done, used)
                    sp.wait_ge(v_done, used)
                sp.dma_start(x2[:, p, :], x_rows[t]).then_inc(rows_in[p], 16)
                sp.dma_start(c2[:, p], ctx_rows[t]).then_inc(rows_in[p], 16)
                sp.dma_start(v2[:, p, :, :], v_cols[t]).then_inc(v_in[p], 16)

            def load_weights(k, p):
                t = 2 * k + p
                used, = worked_out(sp, t)
                sp.wait_ge(consts_in, 64)
                sp.wait_ge(w_lo_done, used)
                sp.dma_start(ws[:], w_all[t]).then_inc(w_in, 16)

            def store_tile(k, p):
                t = 2 * k + p
                ready, = worked_out(sp, 4 * (t + 1))
                sp.wait_ge(consts_in, 64)
                sp.wait_ge(os_done, ready)
                for j in range(JOBS):
                    sp.dma_start(scratch[t, :, j].rearrange("g r n -> r g n"),
                                 os2[32 * j:32 * j + OROWS, p, :, :]).then_inc(stored[p], 16)

            def tile(k, p, first=False, next3=True, next2=True):
                if not first:
                    store_tile(*tile_at(k, p, -1))
                if next3:
                    load_tile(*tile_at(k, p, 3))
                if next2:
                    load_weights(*tile_at(k, p, 2))

            load_tile(0, 0, early=True)
            sp.dma_start(sel_in, select).then_inc(sel_loaded, 16)
            sp.dma_start(ident[:], eye).then_inc(consts_in, 16)
            sp.dma_start(marks[:], row_marks).then_inc(consts_in, 16)
            load_tile(0, 1, early=True)
            sp.dma_start(router_sb[:], router).then_inc(consts_in, 16)
            sp.dma_start(g3[:], gates.partition_broadcast(P)).then_inc(consts_in, 16)
            sp.dma_start(ws[:], w_all[0]).then_inc(w_in, 16)
            load_tile(1, 0)
            load_weights(0, 1)
            tile(0, 0, first=True)
            tile(0, 1)
            with sp.Fori(1, TILES // 2 - 2) as k:
                for p in range(2):
                    tile(k, p)
            tile(TILES // 2 - 2, 0)
            tile(TILES // 2 - 2, 1, next3=False)
            tile(TILES // 2 - 1, 0, next3=False, next2=False)
            tile(TILES // 2 - 1, 1, next3=False, next2=False)
            store_tile(TILES // 2 - 1, 1)
            for p in range(2):
                sp.wait_ge(stored[p], 32 * TILES)

        @block.gpsimd
        def _(pool):
            pool.memset(half[:], -0.5).then_inc(init, 1)
            pool.memset(zero[:], 0.0).then_inc(init, 1)
            pool.memset(vs2[:], 0.0).then_inc(init, 1)
            pool.wait_ge(init, 3)
            pool.memset(vs2[:, :, :, :, DH:2 * DH], 1.0).then_inc(init, 1)
            pool.wait_ge(init, 4)

            def rstd_tile(k, p):
                t = 2 * k + p
                done, = worked_out(pool, t + 1)
                pool.wait_ge(init, 4)
                pool.wait_ge(mv_done, done)
                pool.tensor_scalar(mv[:, p, 1:2], mv[:, p, 1:2], EPS, None, ALU.add).then_inc(veps_done, 1)
                pool.wait_ge(veps_done, done)
                pool.tensor_tensor(rstd[:, p, :], mv[:, p, 1:2], half[:], ALU.pow).then_inc(rstd_done, 1)

            def queries_tile(k, p, early=False):
                t = 2 * k + p
                done, stacked = worked_out(pool, t + 1, 4 * (t - 1))
                pool.wait_ge(init, 4)
                pool.wait_ge(xn_done, done)
                if not early:
                    pool.wait_ge(q_stacked, stacked)
                pool.tensor_scalar(q_hi2[:, p, :], xn[:], 1.0, 0.0, ALU.mult, ALU.add).then_inc(q_hi_done, 1)
                pool.wait_ge(q_hi_done, t + 1)
                pool.tensor_tensor(q_lo2[:, p, :], xn[:], f32(q_hi2[:, p, :]), ALU.subtract).then_inc(q_lo_done, 1)

            def keys_tile(k, p, early=False):
                t = 2 * k + p
                loaded, stacked = worked_out(pool, 32 * (k + 1), 4 * (t - 1))
                pool.wait_ge(init, 4)
                pool.wait_ge(rows_in[p], loaded)
                if not early:
                    pool.wait_ge(k_stacked, stacked)
                pool.tensor_scalar(k_hl2[:, p], c2[:, p], 1.0, 0.0, ALU.mult, ALU.add).then_inc(k_hi_done, 1)
                pool.wait_ge(k_hi_done, t + 1)
                low = slice(HALF, P)
                pool.tensor_tensor(k_hl2[low, p], c2[low, p], f32(k_hl2[low, p]), ALU.subtract).then_inc(k_lo_done, 1)
                pool.wait_ge(k_lo_done, t + 1)

            def weights_tile(k, p):
                t = 2 * k + p
                pool.wait_ge(w_in, 16 * (t + 1))
                cols = bass.ds(t * WSLICE, WSLICE)
                pool.tensor_tensor(w_hi[:, cols], ws[:], zero[:].broadcast_to([P, WSLICE]), ALU.add)\
                    .then_inc(w_hi_done, 1)

            def weights_lo_tile(k, p):
                t = 2 * k + p
                cols = bass.ds(t * WSLICE, WSLICE)
                pool.wait_ge(w_hi_done, t + 1)
                pool.tensor_tensor(w_lo[:, cols], ws[:], f32(w_hi[:, cols]), ALU.subtract)\
                    .then_inc(w_lo_done, 1)

            def values_tile(k, p, early=False):
                t = 2 * k + p
                loaded, used = worked_out(pool, 16 * (k + 1), 4 * (t - 1))
                pool.wait_ge(init, 4)
                pool.wait_ge(v_in[p], loaded)
                if not early:
                    pool.wait_ge(pv_ready, used)
                pool.tensor_scalar(vs2[:, p, :, :, 0:DH],
                                   v2[:, p, :, :].rearrange("k a (h d) -> k a h d", d=DH),
                                   1.0, 0.0, ALU.mult, ALU.add).then_inc(v_done, 1)

            def alone(s, r, early=False):
                done, used = worked_out(pool, s + 1, 2 * (s - RING + 1))
                pool.wait_ge(init, 4)
                pool.wait_ge(ks_done, done)
                if not early:
                    pool.wait_ge(st_ready, used)
                pool.tensor_tensor(ko4[:, r], f32(ks4[:, r, :]).unsqueeze(1).broadcast_to([P, 2, L]),
                                   marks[:, 1:3].unsqueeze(2).broadcast_to([P, 2, L]), ALU.mult).then_inc(ko_done, 1)

            def tile(k, p, next2=True, next1=True, values=True):
                s = 4 * (2 * k + p) + 3
                alone(s, 3, early=values is False)
                if next2:
                    keys_tile(*tile_at(k, p, 2))
                if next1:
                    alone(s + 1, 0)
                    if next2:
                        rstd_tile(*tile_at(k, p, 2))
                    weights_tile(*tile_at(k, p, 1))
                    alone(s + 2, 1)
                    if next2:
                        queries_tile(*tile_at(k, p, 2))
                    if values:
                        values_tile(*tile_at(k, p, 1))
                    alone(s + 3, 2)
                    weights_lo_tile(*tile_at(k, p, 1))

            for p in range(2):
                rstd_tile(0, p)
                keys_tile(0, p, early=True)
                queries_tile(0, p, early=True)
            pool.wait_ge(consts_in, 64)
            for s in range(3):
                alone(s, s, early=True)
            for p in range(2):
                values_tile(0, p, early=True)
            weights_tile(0, 0)
            weights_lo_tile(0, 0)
            tile(0, 0, values=False)
            tile(0, 1)
            with pool.Fori(1, TILES // 2 - 1) as k:
                for p in range(2):
                    tile(k, p)
            tile(TILES // 2 - 1, 0, next2=False)
            tile(TILES // 2 - 1, 1, next2=False, next1=False)

        @block.scalar
        def _(act):
            def exps(s, u, n_slot, early):
                act.wait_ge(st_ready, 2 * s + u + 1)
                if not early:
                    act.wait_ge(pv_ready, s - 1)
                act.activation(pr[:, n_slot], st_ps[u][:], ACT.Exp, scale=SCALE).then_inc(exp_done, 1)

            def results(s, k, g, p, early, stacked):
                if stacked:
                    act.wait_ge(q_stacked, s + RING + 2)
                else:
                    act.wait_ge(pv_ready, s + 1)
                if g == 0 and not early:
                    act.wait_ge(stored[p], 64 * k)
                act.copy(os2[:, p, g, :], pv_ps).then_inc(os_done, 1)

            def stacked_q(s, r, early):
                act.wait_ge(q_stacked, s + 1)
                if not early:
                    act.wait_ge(qm_done, s - RING + 1)
                act.copy(qs4[:, r, :], q_ps).then_inc(qs_done, 1)

            def stacked_k(s, r, early):
                act.wait_ge(k_stacked, s + 1)
                if not early:
                    act.wait_ge(st_ready, 2 * (s - RING + 1))
                act.activation(ks4[:, r, :], k_ps, ACT.Identity, bias=marks[:, 0:1]).then_inc(ks_done, 1)

            def step(s0, d):
                s = s0 + d
                static = isinstance(s0, int)
                more = not (static and s + RING >= STEPS)
                if not (static and not 0 <= s + 3 < STEPS):
                    stacked_k(s + 3, (d + 3) % RING, static and s < 1)
                    stacked_q(s + 3, (d + 3) % RING, static and s < 1)
                if not (static and s < 0):
                    for u in range(2):
                        exps(s, u, 2 * (d % 2) + u, static and s < 2)
                if not (static and s < 1):
                    results(s - 1, k_reg[0] + (d - 1) // 8, (d - 1) % 4, (d - 1) // 4 % 2,
                            static and s - 1 < 8, more)

            act.wait_ge(consts_in, 64)
            k_reg = [0]
            for d in range(-RING, 8):
                step(0, d)
            with act.Fori(1, TILES // 2 - 1) as i:
                k_reg[0] = i
                for d in range(8):
                    step(i * 8, d)
            k_reg[0] = TILES // 2 - 1
            for d in range(8):
                step(STEPS - 8, d)
            results(STEPS - 1, TILES // 2 - 1, GROUPS - 1, 1, False, False)

        @block.vector
        def _(dve):
            def prep_stats(k, p):
                t = 2 * k + p
                dve.wait_ge(rows_in[p], 32 * (k + 1))
                dve.bn_stats(stats[:, p, :], x2[:, p, :]).then_inc(stats_done, 1)
                done, = worked_out(dve, t + 1)
                dve.wait_ge(init, 4)
                dve.wait_ge(stats_done, done)
                dve.bn_aggr(mv[:, p, :], stats[:, p, :]).then_inc(mv_done, 1)

            def prep_norm(k, p, early=False):
                t = 2 * k + p
                dve.wait_ge(rstd_done, t + 1)
                if not early:
                    dve.wait_ge(q_lo_done, t)
                dve.tensor_scalar(xn[:], x2[:, p, :], mv[:, p, 0:1], rstd[:, p, 0:1],
                                  ALU.subtract, ALU.mult).then_inc(xn_done, 1)

            def maxima(s, j, p):
                dve.wait_ge(s_ready, 4 * s + j + 1)
                dve.tensor_reduce(mx[:, p, j, :], s_ps[j % 2][:], AX_X, ALU.max).then_inc(max_done, 1)

            def shifted(s, r, p, early):
                dve.wait_ge(mt_done, s + 1)
                if not early:
                    dve.wait_ge(st_ready, 2 * s - 2)
                dve.tensor_tensor(qm2[:, p, :], f32(qs4[:, r, :]), mt_ps, ALU.add).then_inc(qm_done, 1)

            def column(p, c):
                return mt2[:, p, :, c::32].rearrange("q a j -> q j a")

            def minus_hi(s, p):
                dve.wait_ge(max_done, 4 * s + 4)
                dve.tensor_scalar(column(p, 3), mx[:, p], -1.0, None, ALU.mult).then_inc(mneg_done, 1)

            def minus_lo(s, p):
                dve.wait_ge(mneg_done, s + 1)
                dve.scalar_tensor_tensor(column(p, 7), mx[:, p], -1.0, f32(column(p, 3)),
                                         ALU.mult, ALU.subtract).then_inc(mt_ready, 1)

            def step(s0, d):
                s = s0 + d
                static = isinstance(s0, int)
                k2, p2 = k_reg[0] + 1, d // 4 % 2
                prep = d >= 0 and not (static and s // 4 + 2 >= TILES)
                ahead = not (static and s + 2 >= STEPS)
                for j in range(JOBS):
                    if ahead:
                        maxima(s + 2, j, d % 2)
                    if j == 1 and not (static and (s + 1 < 0 or s + 1 >= STEPS)):
                        shifted(s + 1, (d + 1) % RING, (d + 1) % 2, static and s + 1 < 2)
                if prep and d % 4 == 0:
                    prep_stats(k2, p2)
                if prep and d % 4 == 1:
                    prep_norm(k2, p2)
                if ahead:
                    minus_hi(s + 2, d % 2)
                    minus_lo(s + 2, d % 2)

            prep_stats(0, 0)
            prep_norm(0, 0, early=True)
            dve.wait_ge(sel_loaded, 16)
            dve.tensor_copy(sel[:], sel_in).then_inc(sel_done, 1)
            prep_stats(0, 1)
            prep_norm(0, 1)
            dve.wait_ge(consts_in, 64)
            dve.tensor_copy(ident_r[:], ident[:]).then_inc(sel_done, 1)
            dve.tensor_scalar(mt2[:].rearrange("p a b c -> p (a b) c"),
                              ident[:].unsqueeze(1).broadcast_to([P, 2 * KT, P]), 0.0, None, ALU.mult)\
                .then_inc(mt_zero, 1)
            dve.wait_ge(mt_zero, 1)
            k_reg = [0]
            for d in range(-2, 8):
                step(0, d)
            with dve.Fori(1, TILES // 2 - 1) as i:
                k_reg[0] = i
                for d in range(8):
                    step(i * 8, d)
            k_reg[0] = TILES // 2 - 1
            for d in range(8):
                step(STEPS - 8, d)

        @block.tensor
        def _(pe):
            pe.wait_ge(consts_in, 64)
            pe.wait_ge(sel_done, 2)

            def stack_q(s, d, early):
                g, tp = d % GROUPS, d // GROUPS % 2
                if g == 0:
                    pe.wait_ge(q_lo_done, 2 * (k_reg[0] + d // 8) + tp + 1)
                if early:
                    if s > 0:
                        pe.wait_ge(qs_done, s)
                pe.matmul(q_ps, sel[:, Q_HI + g, :], q_hi2[:, tp, :], start=True, stop=False)
                pe.matmul(q_ps, sel[:, Q_LO + g, :], q_lo2[:, tp, :], start=False, stop=True).then_inc(q_stacked, 1)

            def stack_k(s, d, turned):
                g, tp = d % GROUPS, d // GROUPS % 2
                if g == 0:
                    pe.wait_ge(k_lo_done, 2 * (k_reg[0] + d // 8) + tp + 1)
                if turned:
                    pe.wait_ge(qm_done, s - 2)
                elif not (isinstance(s, int) and s == 0):
                    pe.wait_ge(ks_done, s)
                pe.matmul(k_ps, sel[:, K_BOTH + g % 2, :], k_hl2[:, tp, g // 2, :], start=True, stop=True)\
                    .then_inc(k_stacked, 1)

            def transpose_maxima(s, p, early, stacked):
                pe.wait_ge(mt_ready, s + 1)
                if stacked:
                    pe.wait_ge(ks_done, s + 3)
                if not early:
                    pe.wait_ge(qm_done, s)
                for a in range(KT):
                    last = pe.matmul(turn_ps[:, 0, a * P:(a + 1) * P], mt2[:, p, a, :], ident_r[:],
                                     start=True, stop=True)
                last.then_inc(mt_done, 1)

            def head(j, r):
                if j % 2 == 0:
                    return slice(0, P), ko4[:, r, j // 2, :]
                rows = slice(32 * j, 32 * j + 32)
                return rows, ks4[rows, r, :]

            def scores(s, j, r, early):
                if j == 0:
                    pe.wait_ge(qs_done, s + 1)
                    pe.wait_ge(ks_done, s + 1)
                    pe.wait_ge(ko_done, s + 1)
                if not early:
                    pe.wait_ge(max_done, 4 * s + j - 1)
                rows, k_head = head(j, r)
                for a in range(KT):
                    last = pe.matmul(s_ps[j % 2][:, a, :], qs4[rows, r, a * P:(a + 1) * P], k_head, start=True, stop=True)
                last.then_inc(s_ready, 1)

            def transposed_scores(s, u, r, p, early):
                pe.wait_ge(qm_done, s + 1)
                if not early:
                    pe.wait_ge(exp_done, 2 * s + u - 1)
                for a in range(KT):
                    for j in (2 * u, 2 * u + 1):
                        rows, k_head = head(j, r)
                        last = pe.matmul(st_ps[u][:, j % 2, a, :], k_head[:, a * P:(a + 1) * P],
                                         qm2[rows, p, :], start=True, stop=True)
                last.then_inc(st_ready, 1)

            def sums(s, a, tp, k, g, p, early, stacked):
                if a == 0:
                    pe.wait_ge(exp_done, 2 * s + 2)
                    if g == 0:
                        pe.wait_ge(v_done, 2 * k + tp + 1)
                    if not early:
                        pe.wait_ge(os_done, s)
                    if stacked:
                        pe.wait_ge(qs_done, s + RING + 1)
                for j in range(JOBS):
                    last = pe.matmul(sums_ps[32 * j:32 * j + 32, 0, :], vs2[:, tp, a, 4 * g + j, :],
                                     pr[:, 2 * p + j // 2, j % 2, a, :], start=(a == 0), stop=(a == KT - 1))
                if a == KT - 1:
                    last.then_inc(pv_ready, 1)

            def step(s0, d):
                s = s0 + d
                static = isinstance(s0, int)

                def ahead(j):
                    if not (static and not 0 <= s + 2 < STEPS):
                        scores(s + 2, j, (d + 2) % RING, static and 4 * (s + 2) + j < 2)

                def now(u):
                    if not (static and not 0 <= s < STEPS):
                        transposed_scores(s, u, d % RING, d % 2, static and s < 1)

                def behind(a):
                    if not (static and s < 1):
                        sums(s - 1, a, (d - 1) // 4 % 2, k_reg[0] + (d - 1) // 8, (d - 1) % 4, (d - 1) % 2,
                             static and s - 1 < 1, not (static and s - 1 + RING >= STEPS))

                if not (static and not 0 <= s + 3 < STEPS):
                    stack_k(s + 3, d + 3, not (static and s < 0))
                ahead(0)
                now(0)
                ahead(1)
                now(1)
                if not (static and not 0 <= s + 1 < STEPS):
                    transpose_maxima(s + 1, (d + 1) % 2, static and s + 1 < 1,
                                     not (static and s + 3 >= STEPS))
                ahead(2)
                behind(0)
                ahead(3)
                behind(1)
                if not (static and s + RING >= STEPS):
                    stack_q(s + RING, d + RING, static and s < 1)

            k_reg = [0]
            for d in range(-RING, 8):
                if d == 0:
                    for _ in range(WARM_UP):
                        pe.matmul(st_ps[1][:, 1], sel[:, 0, :], sel[:, 0:4], start=True, stop=True)
                step(0, d)
            with pe.Fori(1, TILES // 2 - 1) as i:
                k_reg[0] = i
                for d in range(8):
                    step(i * 8, d)
            k_reg[0] = TILES // 2 - 1
            for d in range(8):
                step(STEPS - 8, d)
            k_reg[0] = TILES // 2
            step(STEPS, 0)


def ffn_phase(nc, x_rows, scratch, ident, router_sb, g3, consts_in, w_hi, w_lo, out_rows):
    GATE, UP, DOWN = 0, KT * WCOLS, 2 * KT * WCOLS
    SLOTS = CHUNKS
    LAG = 2

    with ExitStack() as ctx:
        def sb(name, shape, dt=F32):
            return ctx.enter_context(nc.sbuf_tensor(name, shape, dt))

        def psum(name, shape):
            return ctx.enter_context(nc.psum_tensor(name, shape, F32))

        def sem(name):
            return ctx.enter_context(nc.semaphore(name))

        r_hl = sb("r_hl", [P, KT, 2, EXPERTS], F32R)
        th = sb("th", [P, 2])
        gx = sb("gx", [P, 1])
        half = sb("f_half", [P, 1])
        xin = sb("xin", [P, BT, L])
        num = sb("num", [P, BT, L])
        den = sb("den", [P, BT, L])
        x1 = sb("x1", [P, 2, BT, L])
        st6 = sb("st6", [P, 6])
        mv = sb("f_mv", [P, 2])
        rstd = sb("f_rstd", [P, 1])
        xn = sb("f_xn", [P, L])
        xh = sb("xh", [P, 2, KT, BLOCK], F32R)
        xl = sb("xl", [P, 2, KT, BLOCK], F32R)
        lg = sb("lg", [P, BT, EXPERTS])
        m8 = sb("m8", [P, 8])
        rep = sb("rep", [P, BT, EXPERTS])
        zz = sb("zz", [P, BT, EXPERTS])
        mask = sb("mask", [P, BT, EXPERTS])
        ez = sb("ez", [P, BT, EXPERTS])
        we = sb("we", [P, BT, EXPERTS])
        wsum = sb("wsum", [P, BT])
        wrec = sb("wrec", [P, BT])
        wx = sb("wx", [P, BT, EXPERTS, 4])
        wb = sb("wb", [P, 2, BLOCK])
        sl = sb("sl", [P, 2, BLOCK])
        su = sb("su", [P, BLOCK])
        hf = sb("hf", [P, 2, BLOCK])
        hh = sb("hh", [P, 3, BLOCK], F32R)
        hl = sb("hl", [P, 3, BLOCK], F32R)
        ot = sb("ot", [P, KT, BLOCK])
        y = sb("y", [P, 2, L])

        g_ps = [psum(f"g_ps{i}", [P, BLOCK]) for i in range(2)]
        u_ps = [psum(f"u_ps{i}", [P, BLOCK]) for i in range(2)]
        acc = [psum(f"acc{i}", [P, BLOCK]) for i in range(KT)]
        last_ps = g_ps + u_ps
        tp = psum("tp", [P, L])
        rt = psum("rt", [P, BLOCK])

        half_set = sem("half_set")
        th_done = sem("th_done")
        gx_done = sem("gx_done")
        rhi_done = sem("rhi_done")
        rlo_done = sem("rlo_done")
        tile_in = [sem(f"tile_in{i}") for i in range(BT)]
        block_in = sem("block_in")
        rec_done = sem("rec_done")
        att_done = sem("att_done")
        x1_done = sem("x1_done")
        st_done = sem("st_done")
        mv_done = sem("f_mv_done")
        veps_done = sem("f_veps_done")
        rstd_done = sem("f_rstd_done")
        xn_done = sem("f_xn_done")
        xt_ready = sem("xt_ready")
        xh_done = sem("xh_done")
        xl_done = sem("xl_done")
        lg_ready = sem("lg_ready")
        lg_done = sem("lg_done")
        m8_done = sem("m8_done")
        rep_done = sem("rep_done")
        z_done = sem("z_done")
        mask_done = sem("mask_done")
        ez_done = sem("ez_done")
        we_done = sem("we_done")
        wsum_done = sem("wsum_done")
        wrec_done = sem("wrec_done")
        wx_done = sem("wx_done")
        wt_ready = sem("wt_ready")
        wb_done = sem("wb_done")
        g_ready = sem("g_ready")
        u_ready = sem("u_ready")
        sl_done = sem("sl_done")
        su_done = sem("su_done")
        hf_done = sem("hf_done")
        hh_done = sem("hh_done")
        hl_done = sem("hl_done")
        down_done = sem("down_done")
        ot_done = sem("ot_done")
        yt_ready = sem("yt_ready")
        y_done = sem("y_done")
        out_done = [sem(f"out_done{i}") for i in range(2)]

        LOADS = 16 * (1 + 2 * BT)

        def blocks(engine, block):
            block(0, 0)
            block(1, 1)
            with engine.Fori(1, BLOCKS // 2 - 1) as m:
                block(m * 2, 0)
                block(m * 2 + 1, 1)
            block(BLOCKS - 2, 0)
            block(BLOCKS - 1, 1)

        def is_first(b):
            return isinstance(b, int) and b == 0

        def is_last(b):
            return isinstance(b, int) and b == BLOCKS - 1

        block_ = ctx.enter_context(nc.Block())

        @block_.sync
        def _(sp):
            def load(b):
                sp.dma_start(xin[:], x_rows[bass.ds(b * BT, BT)].rearrange("t p n -> p t n")).then_inc(block_in, 16)
                for i in range(BT):
                    rows = scratch[b * BT + i].rearrange("g j r n -> (g j) r n")
                    sp.dma_start(num[:, i, :], rows[:, 0:DH, :]).then_inc(block_in, 16)
                    sp.dma_start(den[:, i, :], rows[:, DH:2 * DH, :]).then_inc(block_in, 16)

            def store(b, i):
                ready, = worked_out(sp, b * BT + i + 1)
                sp.wait_ge(consts_in, 64)
                sp.wait_ge(y_done, ready)
                sp.dma_start(out_rows[b * BT + i], y[:, i % 2, :]).then_inc(out_done[i % 2], 16)

            for i in range(BT):
                rows = scratch[i].rearrange("g j r n -> (g j) r n")
                sp.dma_start(den[:, i, :], rows[:, DH:2 * DH, :]).then_inc(tile_in[i], 16)
                sp.dma_start(num[:, i, :], rows[:, 0:DH, :]).then_inc(tile_in[i], 16)
                sp.dma_start(xin[:, i, :], x_rows[i]).then_inc(tile_in[i], 16)
            sp.wait_ge(x1_done, BT)
            load(1)

            def block(b, d):
                if not is_first(b):
                    for i in range(BT):
                        store(b - 1, i)
                if not (is_last(b) or isinstance(b, int) and b == BLOCKS - 2):
                    used, = worked_out(sp, BT * (b + 2))
                    sp.wait_ge(consts_in, 64)
                    sp.wait_ge(x1_done, used)
                    load(b + 2)

            block(0, 0)
            with sp.Fori(1, BLOCKS - 2) as b:
                block(b, None)
            block(BLOCKS - 2, 0)
            block(BLOCKS - 1, 1)
            for i in range(BT):
                sp.wait_ge(y_done, BT * (BLOCKS - 1) + i + 1)
                sp.dma_start(out_rows[BT * (BLOCKS - 1) + i], num[:, i, :]).then_inc(out_done[i % 2], 16)
            for i in range(2):
                sp.wait_ge(out_done[i], 16 * TILES // 2)

        @block_.gpsimd
        def _(pool):
            pool.memset(half[:], -0.5).then_inc(half_set, 1)
            pool.wait_ge(half_set, 1)

            def deviation(n):
                done, = worked_out(pool, n + 1)
                pool.wait_ge(half_set, 1)
                pool.wait_ge(mv_done, done)
                pool.tensor_scalar(mv[:, 1:2], mv[:, 1:2], EPS, None, ALU.add).then_inc(veps_done, 1)
                pool.wait_ge(veps_done, done)
                pool.tensor_tensor(rstd[:], mv[:, 1:2], half[:], ALU.pow).then_inc(rstd_done, 1)

            def attended(b, i):
                done, = worked_out(pool, b * BT + i + 1)
                pool.wait_ge(half_set, 1)
                pool.wait_ge(rec_done, done)
                pool.tensor_tensor(num[:, i, :], num[:, i, :], den[:, i, :], ALU.mult).then_inc(att_done, 1)

            with pool.Fori(0, BLOCKS) as b:
                attended(b, 0)
                for i in range(BT):
                    if i + 1 < BT:
                        attended(b, i + 1)
                    deviation(b * BT + i)

        @block_.scalar
        def _(act):
            act.wait_ge(consts_in, 64)
            act.activation(th[:], g3[:, 0:2], ACT.Tanh).then_inc(th_done, 1)

            def high_tokens(b, d, i):
                act.wait_ge(xt_ready, b * BT + i + 1)
                if not (isinstance(b, int) and b < 2):
                    act.wait_ge(u_ready, CHUNKS * (b - 1))
                act.copy(xh[:, d, :, i * P:i * P + P], tp[:].rearrange("p (k t) -> p k t", k=KT)).then_inc(xh_done, 1)

            def exps(b):
                act.wait_ge(z_done, BT * (b + 1))
                if not is_first(b):
                    act.wait_ge(we_done, b)
                act.activation(ez[:], zz[:], ACT.Exp).then_inc(ez_done, 1)

            def slot(b, c):
                n = b * CHUNKS + c
                early = is_first(b)
                act.wait_ge(g_ready, n + 1)
                if not (early and c < 2):
                    act.wait_ge(su_done, n - 1)
                act.activation(sl[:, c % 2, :], g_ps[c % 2][:], ACT.Silu).then_inc(sl_done, 1)
                act.wait_ge(hf_done, n + 1)
                if not (early and c < 3):
                    act.wait_ge(down_done, n - 2)
                act.copy(hh[:, c % 3, :], hf[:, c % 2, :]).then_inc(hh_done, 1)

            def collect(b):
                act.wait_ge(down_done, CHUNKS * (b + 1))
                if not is_first(b):
                    act.wait_ge(yt_ready, BT * b)
                for k in range(KT):
                    act.copy(ot[:, k, :], acc[k][:]).then_inc(ot_done, 1)

            for i in range(BT):
                high_tokens(0, 0, i)
            exps(0)

            def block(b, d):
                for c in range(SLOTS):
                    if c - 8 in range(0, 2 * BT, 2) and not is_last(b):
                        high_tokens(b + 1, 1 - d, (c - 8) // 2)
                    slot(b, c)
                    if c == LAG - 1 and not is_first(b):
                        collect(b - 1)
                    if c == 18 and not is_last(b):
                        exps(b + 1)

            blocks(act, block)
            collect(BLOCKS - 1)

        @block_.vector
        def _(dve):
            dve.wait_ge(consts_in, 64)
            dve.tensor_copy(r_hl[:, :, 0, :], router_sb[:]).then_inc(rhi_done, 1)
            dve.wait_ge(rhi_done, 1)
            dve.tensor_tensor(r_hl[:, :, 1, :], router_sb[:], f32(r_hl[:, :, 0, :]), ALU.subtract).then_inc(rlo_done, 1)
            dve.wait_ge(th_done, 1)
            dve.tensor_tensor(gx[:], th[:, 0:1], g3[:, 2:3], ALU.mult).then_inc(gx_done, 1)
            dve.wait_ge(gx_done, 1)

            def inverse(b, d, i):
                if is_first(b):
                    dve.wait_ge(tile_in[i], 48)
                else:
                    dve.wait_ge(block_in, LOADS * b)
                dve.reciprocal(den[:, i, :], den[:, i, :]).then_inc(rec_done, 1)

            def residual(b, d, i):
                n = b * BT + i
                dve.wait_ge(att_done, n + 1)
                if not (isinstance(b, int) and b < 2):
                    dve.wait_ge(y_done, n - 2 * BT + 1)
                dve.scalar_tensor_tensor(x1[:, d, i, :], num[:, i, :], gx[:, 0:1], xin[:, i, :],
                                         ALU.mult, ALU.add).then_inc(x1_done, 1)
                dve.wait_ge(x1_done, n + 1)
                if not (is_first(b) and i == 0):
                    dve.wait_ge(mv_done, n)
                dve.bn_stats(st6[:], x1[:, d, i, :]).then_inc(st_done, 1)

            def variance(b, d, i):
                n = b * BT + i
                done, used = worked_out(dve, n + 1, n)
                dve.wait_ge(consts_in, 64)
                dve.wait_ge(st_done, done)
                if not (is_first(b) and i == 0):
                    dve.wait_ge(xn_done, used)
                dve.bn_aggr(mv[:], st6[:]).then_inc(mv_done, 1)

            def normalise(b, d, i):
                n = b * BT + i
                dve.wait_ge(rstd_done, n + 1)
                if not (is_first(b) and i == 0):
                    dve.wait_ge(xt_ready, n)
                dve.tensor_scalar(xn[:], x1[:, d, i, :], mv[:, 0:1], rstd[:, 0:1],
                                  ALU.subtract, ALU.mult).then_inc(xn_done, 1)

            def split_tokens(b, d, i):
                n = b * BT + i
                src = tp[:].rearrange("p (k t) -> p k t", k=KT)
                at = (slice(None), d, slice(None), slice(i * P, i * P + P))
                dve.wait_ge(xh_done, n + 1)
                dve.tensor_tensor(xl[at], src, f32(xh[at]), ALU.subtract).then_inc(xl_done, 1)

            def top8(b, d, i):
                n = b * BT + i
                dve.wait_ge(lg_ready, n + 1)
                if not is_first(b):
                    dve.wait_ge(mask_done, b)
                dve.tensor_reduce(lg[:, i, :], rt[:, 0:2 * EXPERTS].rearrange("p (h e) -> p e h", h=2), AX_X, ALU.add)\
                    .then_inc(lg_done, 1)
                done, used = worked_out(dve, n + 1, n)
                dve.wait_ge(consts_in, 64)
                dve.wait_ge(lg_done, done)
                if not (is_first(b) and i == 0):
                    dve.wait_ge(rep_done, used)
                    dve.wait_ge(z_done, used)
                dve.max(m8[:], lg[:, i, :]).then_inc(m8_done, 1)

            def strike(b, d, i):
                n = b * BT + i
                done, = worked_out(dve, n + 1)
                dve.wait_ge(consts_in, 64)
                dve.wait_ge(m8_done, done)
                dve.match_replace(rep[:, i, :], in_to_replace=m8[:], in_values=lg[:, i, :],
                                  imm_value=-3.0e38).then_inc(rep_done, 1)
                if not is_first(b):
                    dve.wait_ge(ez_done, b)
                dve.tensor_scalar(zz[:, i, :], lg[:, i, :], m8[:, 0:1], None, ALU.subtract).then_inc(z_done, 1)

            def masks(b):
                dve.wait_ge(rep_done, BT * (b + 1))
                if not is_first(b):
                    dve.wait_ge(we_done, b)
                dve.tensor_tensor(mask[:], rep[:], lg[:], ALU.not_equal).then_inc(mask_done, 1)

            def weights(b):
                dve.wait_ge(mask_done, b + 1)
                dve.wait_ge(ez_done, b + 1)
                if not is_first(b):
                    dve.wait_ge(wx_done, BT * b)
                dve.tensor_tensor(we[:], ez[:], mask[:], ALU.mult).then_inc(we_done, 1)
                dve.wait_ge(we_done, b + 1)
                dve.tensor_reduce(wsum[:], we[:], AX_X, ALU.add).then_inc(wsum_done, 1)

            def shares(b):
                dve.wait_ge(wsum_done, b + 1)
                dve.reciprocal(wrec[:], wsum[:]).then_inc(wrec_done, 1)

            def spread(b):
                dve.wait_ge(wrec_done, b + 1)
                if not is_first(b):
                    dve.wait_ge(wt_ready, b)
                for i in range(BT):
                    dve.tensor_scalar(wx[:, i], we[:, i, :].unsqueeze(2).broadcast_to([P, EXPERTS, 4]),
                                      wrec[:, i:i + 1], None, ALU.mult).then_inc(wx_done, 1)

            def routed(b, d):
                dve.wait_ge(wt_ready, b + 1)
                if not (isinstance(b, int) and b < 2):
                    dve.wait_ge(hf_done, CHUNKS * (b - 1))
                dve.tensor_copy(wb[:, d, :], rt[:]).then_inc(wb_done, 1)

            def outputs(b, d, i):
                n = b * BT + i
                dve.wait_ge(yt_ready, n + 1)
                if not (is_first(b) and i < 2):
                    dve.wait_ge(out_done[i % 2], 16 * (b * (BT // 2) + i // 2))
                dve.scalar_tensor_tensor(y[:, i % 2, :], tp[:], th[:, 1:2], x1[:, d, i, :],
                                         ALU.mult, ALU.add).then_inc(y_done, 1)

            def lows(n, c):
                dve.wait_ge(hh_done, n + 1)
                dve.tensor_tensor(hl[:, c % 3, :], hf[:, c % 2, :], f32(hh[:, c % 3, :]), ALU.subtract)\
                    .then_inc(hl_done, 1)

            def slot(b, d, c):
                n = b * CHUNKS + c
                early = is_first(b)
                dve.wait_ge(sl_done, n + 1)
                dve.wait_ge(u_ready, n + 1)
                if not (early and c < 1):
                    dve.wait_ge(hf_done, n)
                dve.tensor_tensor(su[:], sl[:, c % 2, :], u_ps[c % 2][:], ALU.mult).then_inc(su_done, 1)
                if not (early and c < 1):
                    lows(n - 1, c - 1)
                dve.wait_ge(su_done, n + 1)
                if c == 0:
                    dve.wait_ge(wb_done, b + 1)
                if not (early and c < 2):
                    dve.wait_ge(hl_done, n - 1)
                dve.tensor_tensor(hf[:, c % 2, :], su[:], wb[:, d, :], ALU.mult).then_inc(hf_done, 1)

            def jobs(b, d, c):
                if not is_first(b) and 3 <= c < 3 + BT:
                    outputs(b - 1, 1 - d, c - 3)
                if is_last(b):
                    return
                for i in range(BT):
                    at = c - (3 + 2 * i)
                    for when, job in ((0, inverse), (1, residual), (2, variance), (3, normalise),
                                      (5, split_tokens), (7, top8), (8, strike)):
                        if at == when:
                            job(b + 1, 1 - d, i)
                if c == 18:
                    masks(b + 1)
                if c == 19:
                    weights(b + 1)
                if c == 20:
                    shares(b + 1)
                if c == 21:
                    spread(b + 1)
                if c == 23:
                    routed(b + 1, 1 - d)

            jobs_of = ((0, inverse), (1, residual), (2, variance), (3, normalise),
                       (4, split_tokens), (6, top8), (7, strike))
            for turn in range(BT + 7):
                for i in range(BT):
                    for when, job in jobs_of:
                        if turn - i == when:
                            job(0, 0, i)
            masks(0)
            weights(0)
            shares(0)
            spread(0)
            routed(0, 0)

            def block(b, d):
                for c in range(SLOTS):
                    slot(b, d, c)
                    jobs(b, d, c)

            blocks(dve, block)
            lows(BLOCKS * CHUNKS - 1, CHUNKS - 1)
            for i in range(BT):
                dve.wait_ge(yt_ready, BT * (BLOCKS - 1) + i + 1)
                dve.scalar_tensor_tensor(num[:, i, :], last_ps[i][:, 0:L], th[:, 1:2], x1[:, 1, i, :],
                                         ALU.mult, ALU.add).then_inc(y_done, 1)

        @block_.tensor
        def _(pe):
            pe.wait_ge(consts_in, 64)

            def turn_tokens(b, i):
                n = b * BT + i
                pe.wait_ge(xn_done, n + 1)
                if not (isinstance(b, int) and b < 2):
                    pe.wait_ge(y_done, BT * (b - 1))
                if not (is_first(b) and i == 0):
                    pe.wait_ge(xl_done, n)
                for k in range(KT):
                    last = pe.transpose(tp[:, k * P:(k + 1) * P], xn[:, k * P:(k + 1) * P], ident[:])
                last.then_inc(xt_ready, 1)

            def route(b, d, i):
                n = b * BT + i
                pe.wait_ge(xl_done, n + 1)
                if not (is_first(b) and i == 0):
                    pe.wait_ge(lg_done, n)
                    if i == 0:
                        pe.wait_ge(wb_done, b)
                terms = [(k, a) for k in range(KT) for a in (xh, xl)]
                for m, (k, a) in enumerate(terms):
                    last = pe.matmul(rt[:, 0:2 * EXPERTS], a[:, d, k, i * P:i * P + P],
                                     r_hl[:, k].rearrange("p h e -> p (h e)"),
                                     start=(m == 0), stop=(m == len(terms) - 1))
                last.then_inc(lg_ready, 1)

            def turn_weights(b):
                pe.wait_ge(wx_done, BT * (b + 1))
                pe.wait_ge(lg_done, BT * (b + 1))
                for i in range(BT):
                    last = pe.transpose(rt[:, i * P:i * P + P], wx[:, i].rearrange("t e r -> t (e r)"), ident[:])
                last.then_inc(wt_ready, 1)

            def turn_outputs(b, i, alone=False):
                n = b * BT + i
                place = last_ps[i] if alone else tp
                if i == 0:
                    pe.wait_ge(ot_done, KT * (b + 1))
                    if not alone:
                        pe.wait_ge(xl_done, BT * (b + 2))
                elif not alone:
                    pe.wait_ge(y_done, n)
                for k in range(KT):
                    last = pe.transpose(place[:, k * P:(k + 1) * P], ot[:, k, i * P:i * P + P], ident[:])
                last.then_inc(yt_ready, 1)

            def gate_or_up(ps, at, c, d):
                for k in range(KT):
                    col = at + (k * CHUNKS + c) * P
                    for w, x in ((w_hi, xh), (w_hi, xl), (w_lo, xh)):
                        last = pe.matmul(ps[:], w[:, col:col + P], x[:, d, k, :],
                                         start=(k == 0 and w is w_hi and x is xh),
                                         stop=(k == KT - 1 and w is w_lo))
                return last

            def down(n, c):
                pe.wait_ge(hl_done, n + 1)
                for k in range(KT):
                    col = DOWN + c * L + k * P
                    for w, h in ((w_hi, hh), (w_hi, hl), (w_lo, hh)):
                        last = pe.matmul(acc[k][:], w[:, col:col + P], h[:, c % 3, :],
                                         start=(c == 0 and w is w_hi and h is hh),
                                         stop=(c == CHUNKS - 1 and w is w_lo))
                last.then_inc(down_done, 1)

            def slot(b, d, c):
                n = b * CHUNKS + c
                early = is_first(b)
                if c == 0:
                    pe.wait_ge(xl_done, BT * (b + 1))
                if not (early and c < 2):
                    pe.wait_ge(sl_done, n - 1)
                gate_or_up(g_ps[c % 2], GATE, c, d).then_inc(g_ready, 1)
                if not (early and c < 2):
                    pe.wait_ge(su_done, n - 1)
                gate_or_up(u_ps[c % 2], UP, c, d).then_inc(u_ready, 1)
                if c == LAG and not early:
                    pe.wait_ge(ot_done, KT * b)
                if not (early and c < LAG):
                    down(n - LAG, (c - LAG) % CHUNKS)

            def jobs(b, d, c):
                if is_first(b) and c == 1:
                    turn_weights(0)
                if not is_first(b) and 3 <= c < 3 + BT:
                    turn_outputs(b - 1, c - 3)
                if is_last(b):
                    return
                for i in range(BT):
                    at = c - (3 + 2 * i)
                    if at == 4:
                        turn_tokens(b + 1, i)
                    if at == 6:
                        route(b + 1, 1 - d, i)
                if c == 22:
                    turn_weights(b + 1)

            turn_tokens(0, 0)
            pe.wait_ge(rlo_done, 1)
            for i in range(BT):
                if i + 1 < BT:
                    turn_tokens(0, i + 1)
                route(0, 0, i)

            def block(b, d):
                for c in range(SLOTS):
                    slot(b, d, c)
                    jobs(b, d, c)

            blocks(pe, block)
            for c in range(LAG):
                down((BLOCKS - 1) * CHUNKS + CHUNKS - LAG + c, CHUNKS - LAG + c)
            for i in range(BT):
                turn_outputs(BLOCKS - 1, i, alone=True)


def flamingo_block(nc, x_rows, ctx_rows, v_cols, w_all, row_marks, select, eye, router, gates, out_rows):
    scratch = nc.dram_tensor("attended", (TILES, GROUPS, JOBS, OROWS, L), F32).ap()
    with ExitStack() as ctx:
        w_hi = ctx.enter_context(nc.sbuf_tensor("w_hi", [P, WALL], F32R))
        w_lo = ctx.enter_context(nc.sbuf_tensor("w_lo", [P, WALL], F32R))
        ident = ctx.enter_context(nc.sbuf_tensor("ident", [P, P], F32))
        router_sb = ctx.enter_context(nc.sbuf_tensor("router_sb", [P, KT, EXPERTS], F32))
        g3 = ctx.enter_context(nc.sbuf_tensor("g3", [P, 3], F32))
        consts_in = ctx.enter_context(nc.semaphore("consts_in"))
        attention_phase(nc, x_rows, ctx_rows, v_cols, w_all, row_marks, select, eye, router, gates,
                        ident, router_sb, g3, consts_in, w_hi, w_lo, scratch)
        ffn_phase(nc, x_rows, scratch, ident, router_sb, g3, consts_in, w_hi, w_lo, out_rows)


def kernel(x, ctx_2048, g_xattn, g_ffn, L0_xattn_gamma, L0_ffn_gate_w, L0_ffn_w_gate_proj,
           L0_ffn_w_up_proj, L0_ffn_w_down_proj):
    import numpy as np
    import concourse.bacc as bacc
    from concourse.bass_utils import run_bass_kernel_spmd

    x, ctx = np.asarray(x), np.asarray(ctx_2048)

    def into_hidden(w):
        w = np.asarray(w).reshape(EXPERTS, 4, CHUNKS, KT, P)
        return w.transpose(4, 3, 2, 0, 1).reshape(P, KT * WCOLS)

    down = np.asarray(L0_ffn_w_down_proj).reshape(EXPERTS, L, 4, CHUNKS)
    down = down.transpose(0, 2, 3, 1).reshape(P, KT * WCOLS)
    w_all = np.concatenate([into_hidden(L0_ffn_w_gate_proj), into_hidden(L0_ffn_w_up_proj), down], axis=1)
    marks = np.zeros((P, 3), np.float32)
    marks[3::32, 0] = marks[7::32, 0] = 1.0
    marks[0:32, 1] = marks[64:96, 2] = 1.0
    select = np.zeros((P, SELECTIONS, P), np.float32)
    for row in range(P):
        group, out = row // 32, row % 32 * 4
        select[row, group, out] = select[row, group, out + 2] = 1.0
        select[row, GROUPS + group, out + 1] = 1.0
        which, out = 2 * GROUPS + row % 64 // 32, row % 32 * 4
        if row < 64:
            select[row, which, out] = select[row, which, out + 1] = 1.0
        else:
            select[row, which, out + 2] = 1.0
    arrays = {
        "x_rows": x.reshape(TILES, P, L),
        "ctx_rows": np.tile(ctx.reshape(TILES, 2, CH, L).transpose(0, 2, 1, 3), (1, 2, 1, 1)),
        "v_cols": ctx.reshape(TILES, P, KT, P).transpose(0, 3, 2, 1),
        "w_all": w_all.reshape(P, TILES, WSLICE).transpose(1, 0, 2),
        "row_marks": marks,
        "select": select,
        "eye": np.eye(P, dtype=np.float32),
        "router": np.asarray(L0_ffn_gate_w).reshape(EXPERTS, KT, P).transpose(2, 1, 0),
        "gates": np.concatenate([np.asarray(g).reshape(1) for g in (g_xattn, g_ffn, L0_xattn_gamma)]),
    }
    arrays = {"in_" + name: np.ascontiguousarray(a) for name, a in arrays.items()}
    nc = bacc.Bacc("TRN2", target_bir_lowering=False, num_devices=1, dynamic_dma_scratch_size=1024)
    args = [nc.dram_tensor(name, a.shape, mybir.dt.from_np(a.dtype), kind="ExternalInput").ap()
            for name, a in arrays.items()]
    out = nc.dram_tensor("out_rows", (TILES, P, L), F32, kind="ExternalOutput").ap()
    flamingo_block(nc, *args, out)
    r = run_bass_kernel_spmd(nc, [arrays], core_ids=[0])
    return r.results[0]["out_rows"].reshape(BATCH, CH, L)
```
